# Optimizing a Trainium2 kernel written in Bass

```python
import numpy as np
import jax
import jax.numpy as jnp

def _softmax(x, axis=-1):
    return jax.nn.softmax(x, axis=axis)

def _gelu(x):
    return jax.nn.gelu(x, approximate=True)

def _silu(x):
    return jax.nn.silu(x)

def _sigmoid(x):
    return jax.nn.sigmoid(x)

def _layernorm(x, axis=-1, eps=1e-05):
    m = jnp.mean(x, axis=axis, keepdims=True)
    v = jnp.var(x, axis=axis, keepdims=True)
    return (x - m) / jnp.sqrt(v + eps)

def _scatter_add(tgt, idx, src, axis=0):
    return tgt.at[idx].add(src)

def _segment_sum(src, seg, n):
    return jax.ops.segment_sum(src, seg, n)
kernel_name = 'mk_dlrm_tower_d1_rec_r8_994714'

def setup_inputs(seed: int=0):
    np.random.seed(seed)
    _w = jnp.asarray

    def _rec_inputs():
        import jax
        import jax.numpy as jnp
        _tk = jax.random.key(seed)
        dense_ctx = jax.random.normal(jax.random.fold_in(_tk, 190), (1024, 16), jnp.float32)
        ids = jnp.stack([jax.random.randint(jax.random.fold_in(_tk, 200 + f), (1024,), 0, v, jnp.int32) for f, v in enumerate([12500, 125000, 1250, 1250, 125000, 1250, 1000, 12500, 12500, 1000, 1250, 12500, 1250, 12500, 125000, 1250, 12500, 12500, 1000, 1000, 1000, 125000, 1250, 1000, 12500, 125000, 1000, 12500, 125000, 1250, 1250, 125000, 1000, 12500, 125000, 1250, 1250, 1000, 1000])], axis=1)
        tbl_0 = 0.05 * jax.random.normal(jax.random.fold_in(_tk, 500 + 0), (12500, 16), jnp.float32)
        tbl_1 = 0.05 * jax.random.normal(jax.random.fold_in(_tk, 500 + 1), (125000, 16), jnp.float32)
        tbl_2 = 0.05 * jax.random.normal(jax.random.fold_in(_tk, 500 + 2), (1250, 16), jnp.float32)
        tbl_3 = 0.05 * jax.random.normal(jax.random.fold_in(_tk, 500 + 3), (1250, 16), jnp.float32)
        tbl_4 = 0.05 * jax.random.normal(jax.random.fold_in(_tk, 500 + 4), (125000, 16), jnp.float32)
        tbl_5 = 0.05 * jax.random.normal(jax.random.fold_in(_tk, 500 + 5), (1250, 16), jnp.float32)
        tbl_6 = 0.05 * jax.random.normal(jax.random.fold_in(_tk, 500 + 6), (1000, 16), jnp.float32)
        tbl_7 = 0.05 * jax.random.normal(jax.random.fold_in(_tk, 500 + 7), (12500, 16), jnp.float32)
        tbl_8 = 0.05 * jax.random.normal(jax.random.fold_in(_tk, 500 + 8), (12500, 16), jnp.float32)
        tbl_9 = 0.05 * jax.random.normal(jax.random.fold_in(_tk, 500 + 9), (1000, 16), jnp.float32)
        tbl_10 = 0.05 * jax.random.normal(jax.random.fold_in(_tk, 500 + 10), (1250, 16), jnp.float32)
        tbl_11 = 0.05 * jax.random.normal(jax.random.fold_in(_tk, 500 + 11), (12500, 16), jnp.float32)
        tbl_12 = 0.05 * jax.random.normal(jax.random.fold_in(_tk, 500 + 12), (1250, 16), jnp.float32)
        tbl_13 = 0.05 * jax.random.normal(jax.random.fold_in(_tk, 500 + 13), (12500, 16), jnp.float32)
        tbl_14 = 0.05 * jax.random.normal(jax.random.fold_in(_tk, 500 + 14), (125000, 16), jnp.float32)
        tbl_15 = 0.05 * jax.random.normal(jax.random.fold_in(_tk, 500 + 15), (1250, 16), jnp.float32)
        tbl_16 = 0.05 * jax.random.normal(jax.random.fold_in(_tk, 500 + 16), (12500, 16), jnp.float32)
        tbl_17 = 0.05 * jax.random.normal(jax.random.fold_in(_tk, 500 + 17), (12500, 16), jnp.float32)
        tbl_18 = 0.05 * jax.random.normal(jax.random.fold_in(_tk, 500 + 18), (1000, 16), jnp.float32)
        tbl_19 = 0.05 * jax.random.normal(jax.random.fold_in(_tk, 500 + 19), (1000, 16), jnp.float32)
        tbl_20 = 0.05 * jax.random.normal(jax.random.fold_in(_tk, 500 + 20), (1000, 16), jnp.float32)
        tbl_21 = 0.05 * jax.random.normal(jax.random.fold_in(_tk, 500 + 21), (125000, 16), jnp.float32)
        tbl_22 = 0.05 * jax.random.normal(jax.random.fold_in(_tk, 500 + 22), (1250, 16), jnp.float32)
        tbl_23 = 0.05 * jax.random.normal(jax.random.fold_in(_tk, 500 + 23), (1000, 16), jnp.float32)
        tbl_24 = 0.05 * jax.random.normal(jax.random.fold_in(_tk, 500 + 24), (12500, 16), jnp.float32)
        tbl_25 = 0.05 * jax.random.normal(jax.random.fold_in(_tk, 500 + 25), (125000, 16), jnp.float32)
        tbl_26 = 0.05 * jax.random.normal(jax.random.fold_in(_tk, 500 + 26), (1000, 16), jnp.float32)
        tbl_27 = 0.05 * jax.random.normal(jax.random.fold_in(_tk, 500 + 27), (12500, 16), jnp.float32)
        tbl_28 = 0.05 * jax.random.normal(jax.random.fold_in(_tk, 500 + 28), (125000, 16), jnp.float32)
        tbl_29 = 0.05 * jax.random.normal(jax.random.fold_in(_tk, 500 + 29), (1250, 16), jnp.float32)
        tbl_30 = 0.05 * jax.random.normal(jax.random.fold_in(_tk, 500 + 30), (1250, 16), jnp.float32)
        tbl_31 = 0.05 * jax.random.normal(jax.random.fold_in(_tk, 500 + 31), (125000, 16), jnp.float32)
        tbl_32 = 0.05 * jax.random.normal(jax.random.fold_in(_tk, 500 + 32), (1000, 16), jnp.float32)
        tbl_33 = 0.05 * jax.random.normal(jax.random.fold_in(_tk, 500 + 33), (12500, 16), jnp.float32)
        tbl_34 = 0.05 * jax.random.normal(jax.random.fold_in(_tk, 500 + 34), (125000, 16), jnp.float32)
        tbl_35 = 0.05 * jax.random.normal(jax.random.fold_in(_tk, 500 + 35), (1250, 16), jnp.float32)
        tbl_36 = 0.05 * jax.random.normal(jax.random.fold_in(_tk, 500 + 36), (1250, 16), jnp.float32)
        tbl_37 = 0.05 * jax.random.normal(jax.random.fold_in(_tk, 500 + 37), (1000, 16), jnp.float32)
        tbl_38 = 0.05 * jax.random.normal(jax.random.fold_in(_tk, 500 + 38), (1000, 16), jnp.float32)
        _rk = jax.random.fold_in(_tk, 7)
        W_top1 = 0.0606339 * jax.random.normal(jax.random.fold_in(_tk, 801), (272, 512), jnp.float32)
        W_top2 = 0.0441942 * jax.random.normal(jax.random.fold_in(_tk, 802), (512, 256), jnp.float32)
        W_top3 = 0.0625 * jax.random.normal(jax.random.fold_in(_tk, 803), (256, 1), jnp.float32)
        b_top1 = jnp.zeros((512,), jnp.float32)
        b_top2 = jnp.zeros((256,), jnp.float32)
        return (dense_ctx, ids, tbl_0, tbl_1, tbl_2, tbl_3, tbl_4, tbl_5, tbl_6, tbl_7, tbl_8, tbl_9, tbl_10, tbl_11, tbl_12, tbl_13, tbl_14, tbl_15, tbl_16, tbl_17, tbl_18, tbl_19, tbl_20, tbl_21, tbl_22, tbl_23, tbl_24, tbl_25, tbl_26, tbl_27, tbl_28, tbl_29, tbl_30, tbl_31, tbl_32, tbl_33, tbl_34, tbl_35, tbl_36, tbl_37, tbl_38, W_top1, b_top1, W_top2, b_top2, W_top3)
    dense_ctx, ids, tbl_0, tbl_1, tbl_2, tbl_3, tbl_4, tbl_5, tbl_6, tbl_7, tbl_8, tbl_9, tbl_10, tbl_11, tbl_12, tbl_13, tbl_14, tbl_15, tbl_16, tbl_17, tbl_18, tbl_19, tbl_20, tbl_21, tbl_22, tbl_23, tbl_24, tbl_25, tbl_26, tbl_27, tbl_28, tbl_29, tbl_30, tbl_31, tbl_32, tbl_33, tbl_34, tbl_35, tbl_36, tbl_37, tbl_38, W_top1, b_top1, W_top2, b_top2, W_top3 = _rec_inputs()

    def _L0_rec_setup():
        import jax, jax.numpy as jnp
        import numpy as np
        B, F0, D = (256, 39, 16)
        LAYER_SIZES = [128, 128, 128]
        key = jax.random.key(seed)
        ks = jax.random.split(key, 1 + 2 * len(LAYER_SIZES))
        inputs = jax.random.normal(ks[0], (B, F0, D), dtype=jnp.float32)
        out = {'inputs': inputs}
        field_nums = [F0]
        for i, size in enumerate(LAYER_SIZES):
            fk = field_nums[-1]
            fan_in = F0 * fk
            scale = np.sqrt(2.0 / (fan_in + size)).astype(np.float32)
            out[f'w{i}'] = jax.random.normal(ks[1 + 2 * i], (F0, fk, size), dtype=jnp.float32) * scale
            out[f'b{i}'] = jnp.zeros((size,), dtype=jnp.float32)
            field_nums.append(size // 2)
        return out
    _L0_rec_all = _L0_rec_setup()
    _L0_rec_in = {k: v for k, v in _L0_rec_all.items() if k in ('w0', 'w1', 'w2', 'b0', 'b1', 'b2')}
    del _L0_rec_all
    return {'dense_ctx': dense_ctx, 'ids': ids, 'tbl_0': tbl_0, 'tbl_1': tbl_1, 'tbl_2': tbl_2, 'tbl_3': tbl_3, 'tbl_4': tbl_4, 'tbl_5': tbl_5, 'tbl_6': tbl_6, 'tbl_7': tbl_7, 'tbl_8': tbl_8, 'tbl_9': tbl_9, 'tbl_10': tbl_10, 'tbl_11': tbl_11, 'tbl_12': tbl_12, 'tbl_13': tbl_13, 'tbl_14': tbl_14, 'tbl_15': tbl_15, 'tbl_16': tbl_16, 'tbl_17': tbl_17, 'tbl_18': tbl_18, 'tbl_19': tbl_19, 'tbl_20': tbl_20, 'tbl_21': tbl_21, 'tbl_22': tbl_22, 'tbl_23': tbl_23, 'tbl_24': tbl_24, 'tbl_25': tbl_25, 'tbl_26': tbl_26, 'tbl_27': tbl_27, 'tbl_28': tbl_28, 'tbl_29': tbl_29, 'tbl_30': tbl_30, 'tbl_31': tbl_31, 'tbl_32': tbl_32, 'tbl_33': tbl_33, 'tbl_34': tbl_34, 'tbl_35': tbl_35, 'tbl_36': tbl_36, 'tbl_37': tbl_37, 'tbl_38': tbl_38, 'W_top1': W_top1, 'b_top1': b_top1, 'W_top2': W_top2, 'b_top2': b_top2, 'W_top3': W_top3, 'L0_rec_w0': _L0_rec_in['w0'], 'L0_rec_w1': _L0_rec_in['w1'], 'L0_rec_w2': _L0_rec_in['w2'], 'L0_rec_b0': _L0_rec_in['b0'], 'L0_rec_b1': _L0_rec_in['b1'], 'L0_rec_b2': _L0_rec_in['b2']}

def reference(dense_ctx, ids, tbl_0, tbl_1, tbl_2, tbl_3, tbl_4, tbl_5, tbl_6, tbl_7, tbl_8, tbl_9, tbl_10, tbl_11, tbl_12, tbl_13, tbl_14, tbl_15, tbl_16, tbl_17, tbl_18, tbl_19, tbl_20, tbl_21, tbl_22, tbl_23, tbl_24, tbl_25, tbl_26, tbl_27, tbl_28, tbl_29, tbl_30, tbl_31, tbl_32, tbl_33, tbl_34, tbl_35, tbl_36, tbl_37, tbl_38, W_top1, b_top1, W_top2, b_top2, W_top3, L0_rec_w0, L0_rec_w1, L0_rec_w2, L0_rec_b0, L0_rec_b1, L0_rec_b2):
    import jax
    import jax.numpy as jnp

    def _L0_rec_ref(inputs, w0, w1, w2, b0, b1, b2):
        import jax, jax.numpy as jnp
        import numpy as np
        B, F0, D = (256, 39, 16)
        LAYER_SIZES = [128, 128, 128]
        x0 = inputs
        xk = inputs
        params = [(w0, b0), (w1, b1), (w2, b2)]
        n_layers = len(params)
        direct = []
        for idx, (W, b) in enumerate(params):
            z = jnp.einsum('bhd,bkd,hks->bsd', x0, xk, W) + b[None, :, None]
            z = jax.nn.relu(z)
            if idx != n_layers - 1:
                half = z.shape[1] // 2
                xk = z[:, :half, :]
                direct.append(z[:, half:, :])
            else:
                direct.append(z)
        logit = jnp.sum(jnp.concatenate(direct, axis=1), axis=-1)
        return logit
    e = jnp.stack([tbl_0[ids[:, 0]], tbl_1[ids[:, 1]], tbl_2[ids[:, 2]], tbl_3[ids[:, 3]], tbl_4[ids[:, 4]], tbl_5[ids[:, 5]], tbl_6[ids[:, 6]], tbl_7[ids[:, 7]], tbl_8[ids[:, 8]], tbl_9[ids[:, 9]], tbl_10[ids[:, 10]], tbl_11[ids[:, 11]], tbl_12[ids[:, 12]], tbl_13[ids[:, 13]], tbl_14[ids[:, 14]], tbl_15[ids[:, 15]], tbl_16[ids[:, 16]], tbl_17[ids[:, 17]], tbl_18[ids[:, 18]], tbl_19[ids[:, 19]], tbl_20[ids[:, 20]], tbl_21[ids[:, 21]], tbl_22[ids[:, 22]], tbl_23[ids[:, 23]], tbl_24[ids[:, 24]], tbl_25[ids[:, 25]], tbl_26[ids[:, 26]], tbl_27[ids[:, 27]], tbl_28[ids[:, 28]], tbl_29[ids[:, 29]], tbl_30[ids[:, 30]], tbl_31[ids[:, 31]], tbl_32[ids[:, 32]], tbl_33[ids[:, 33]], tbl_34[ids[:, 34]], tbl_35[ids[:, 35]], tbl_36[ids[:, 36]], tbl_37[ids[:, 37]], tbl_38[ids[:, 38]]], axis=1)
    z = _L0_rec_ref(e, L0_rec_w0, L0_rec_w1, L0_rec_w2, L0_rec_b0, L0_rec_b1, L0_rec_b2)
    z = z.reshape(z.shape[0], -1)
    h = jnp.concatenate([z, dense_ctx], axis=1)
    h = jnp.maximum(h @ W_top1 + b_top1, 0.0)
    h = jnp.maximum(h @ W_top2 + b_top2, 0.0)
    y = h @ W_top3
    return y

_drawn_inputs = setup_inputs


def setup_inputs(seed=0):
    import zlib

    import numpy as np

    out = dict(_drawn_inputs(seed))
    spreads = {'b_top1': (0.0, 2.0),
     'b_top2': (0.0, 2.0),
     'L0_rec_b0': (0.0, 0.34),
     'L0_rec_b1': (0.0, 0.534),
     'L0_rec_b2': (0.0, 0.8)}
    factors = {'tbl_0': 8.0,
     'tbl_1': 8.0,
     'tbl_2': 8.0,
     'tbl_3': 8.0,
     'tbl_4': 8.0,
     'tbl_5': 8.0,
     'tbl_6': 8.0,
     'tbl_7': 8.0,
     'tbl_8': 8.0,
     'tbl_9': 8.0,
     'tbl_10': 8.0,
     'tbl_11': 8.0,
     'tbl_12': 8.0,
     'tbl_13': 8.0,
     'tbl_14': 8.0,
     'tbl_15': 8.0,
     'tbl_16': 8.0,
     'tbl_17': 8.0,
     'tbl_18': 8.0,
     'tbl_19': 8.0,
     'tbl_20': 8.0,
     'tbl_21': 8.0,
     'tbl_22': 8.0,
     'tbl_23': 8.0,
     'tbl_24': 8.0,
     'tbl_25': 8.0,
     'tbl_26': 8.0,
     'tbl_27': 8.0,
     'tbl_28': 8.0,
     'tbl_29': 8.0,
     'tbl_30': 8.0,
     'tbl_31': 8.0,
     'tbl_32': 8.0,
     'tbl_33': 8.0,
     'tbl_34': 8.0,
     'tbl_35': 8.0,
     'tbl_36': 8.0,
     'tbl_37': 8.0,
     'tbl_38': 8.0,
     'L0_rec_w0': 8.0,
     'L0_rec_w1': 6.306,
     'L0_rec_w2': 4.787,
     'dense_ctx': 8.0}
    for name, (base, spread) in spreads.items():
        noise = np.random.default_rng([zlib.crc32(name.encode()), seed]).standard_normal(out[name].shape)
        drawn = base * np.exp(spread * noise) if base else spread * noise
        out[name] = jnp.asarray(drawn.astype(out[name].dtype))
    for name, factor in factors.items():
        out[name] = (out[name] * factor).astype(out[name].dtype)
    return out
```

```python
from contextlib import ExitStack

import numpy as np

import concourse.bass as bass
from concourse import mybir

BATCH, FIELDS, DIM, DENSE = 1024, 39, 16, 16
SIZE = 128
HALF = SIZE // 2
HID1, HID2 = 512, 256
ST = 128
SAMPLE_TILES = BATCH // ST
COLS = 512
CT = ST * DIM // COLS
COLUMN_TILES = SAMPLE_TILES * CT
PARTS = 3
STACK = PARTS * FIELDS
DISTANCES = (FIELDS - 1) // 2
PAIR_BLOCKS = 3
PAIR_ROWS = PAIR_BLOCKS * FIELDS
PAIR_CHUNKS = -(-(DISTANCES + 1) // PAIR_BLOCKS)
PAIR_TAIL = (DISTANCES + 1 - PAIR_BLOCKS * (PAIR_CHUNKS - 1)) * FIELDS
ROWS = FIELDS * HALF
CHUNKS = -(-ROWS // 128)
TAIL = ROWS - 128 * (CHUNKS - 1)
GROUP = 4
GROUPS = CHUNKS // GROUP
SPLIT = (1, 2, 3)
NSPLIT = len(SPLIT)
WHOLE = tuple(g for g in range(GROUPS) if g not in SPLIT)
PAIR_GROUPS = ((0, 4), (4, PAIR_CHUNKS))
OPERANDS = PAIR_CHUNKS + 1
OP_ITEMS = OPERANDS // 2
BC_ITEMS = CHUNKS // 2
RING = 4
SPLIT_RING = 2

SLOTS = ([(1, g) for g in range(GROUPS)] + [(0, g) for g in range(len(PAIR_GROUPS))]
         + [(2, g) for g in range(GROUPS)])
SPLIT_SLOTS = [s for s, (layer, g) in enumerate(SLOTS) if layer and g in SPLIT]
END1 = GROUPS - 1
END0 = GROUPS + len(PAIR_GROUPS) - 1
END2 = len(SLOTS) - 1
PART_STEPS = (END1 + 2, END1 + 4, END1 + 6)
PER_TILE = {0: len(PAIR_GROUPS), 1: GROUPS, 2: GROUPS}
GATHERS = FIELDS // (CT - 1)


def ahead(layer):
    return 1 if layer == 0 else 0


def exists(j, s):
    tile = j + ahead(SLOTS[s][0])
    return 0 <= tile < COLUMN_TILES and (SLOTS[s][0] == 0 or j >= 0)


def user_before(j, s, known):
    back = s - RING
    while True:
        off, slot = (0, back) if back >= 0 else (-1, back + len(SLOTS))
        if not known or exists(j + off, slot):
            return off, slot
        back -= RING
        if back < -len(SLOTS):
            return None


def split_before(j, i, known):
    back = i - SPLIT_RING
    off, k = (0, back) if back >= 0 else (-1, back + len(SPLIT_SLOTS))
    if known and not exists(j + off, SPLIT_SLOTS[k]):
        return None
    return off, SPLIT_SLOTS[k]


def build(nc, dense, ids, tables, w0_fwd, w0_rev, w1, w2, w_top1, w_top2, columns, select, identity, out):
    f32, f32r, bf16, i32 = mybir.dt.float32, mybir.dt.float32r, mybir.dt.bfloat16, mybir.dt.int32
    ACT, ALU = mybir.ActivationFunctionType, mybir.AluOpType

    with ExitStack() as ctx:
        def sb(name, shape, dt=f32):
            return ctx.enter_context(nc.sbuf_tensor(name, shape, dt))

        def ps(name, shape):
            return ctx.enter_context(nc.psum_tensor(name, shape, f32))

        def sem(name):
            return ctx.enter_context(nc.semaphore(name))

        select_sb = sb("select_sb", [STACK, OPERANDS + CHUNKS, 128], bf16)
        identity_sb = sb("identity_sb", [128, 128], bf16)
        w0_sb = sb("w0_sb", [PAIR_ROWS, PAIR_CHUNKS, SIZE])
        w_whole = {1: sb("w1_whole", [128, len(WHOLE) * GROUP, SIZE]), 2: sb("w2_whole", [128, len(WHOLE) * GROUP, SIZE])}
        w_high = {1: sb("w1_high", [128, NSPLIT * GROUP, SIZE], f32r), 2: sb("w2_high", [128, NSPLIT * GROUP, SIZE], f32r)}
        w_low = {1: sb("w1_low", [128, NSPLIT * GROUP, SIZE], f32r), 2: sb("w2_low", [128, NSPLIT * GROUP, SIZE], f32r)}
        columns_sb = sb("columns_sb", [128, 3 + HID1 // 128 + 2 * (HID2 // 128)])
        bias_sb = columns_sb[:, 0:3]
        bias_top1_sb = columns_sb[:, 3:3 + HID1 // 128]
        bias_top2_sb = columns_sb[:, 3 + HID1 // 128:3 + HID1 // 128 + HID2 // 128]
        top3_sb = columns_sb[:, 3 + HID1 // 128 + HID2 // 128:]
        top1_sb = sb("top1_sb", [128, 2, HID1])
        top1_dense_sb = sb("top1_dense_sb", [DENSE, HID1])
        top2_sb = sb("top2_sb", [128, HID1 // 128, HID2])
        index_sb = sb("index_sb", [ST, FIELDS], i32)
        rows_sb = sb("rows_sb", [ST, FIELDS, DIM])
        rest_sb = sb("rest_sb", [ST, DIM, FIELDS])
        parts_sb = sb("parts_sb", [ST, DIM, PARTS, FIELDS], bf16)
        stacked = sb("stacked", [STACK, CT, COLS], bf16)
        pair_ops = sb("pair_ops", [128, OPERANDS, COLS])
        x0_rows = sb("x0_rows", [128, CHUNKS, COLS])
        x1_rows = sb("x1_rows", [128, COLS])
        x2_rows = sb("x2_rows", [128, COLS])
        products = sb("products", [128, RING, GROUP, COLS])
        prod_high = sb("prod_high", [128, SPLIT_RING, GROUP, COLS], f32r)
        prod_low = sb("prod_low", [128, SPLIT_RING, GROUP, COLS], f32r)
        direct01 = sb("direct01", [128, 2, COLS])
        direct2 = sb("direct2", [128, 2, COLS])
        half_sum = sb("half_sum", [128, 2, COLS // 2])
        tile_sum = sb("tile_sum", [128, 2, ST])
        running = sb("running", [128, 2, ST])
        features = sb("features", [128, 2, ST])
        dense_sb = sb("dense_sb", [DENSE, ST])
        hidden1 = sb("hidden1", [128, HID1 // 128, ST])
        hidden2 = sb("hidden2", [128, HID2 // 128, ST])
        y_sb = sb("y_sb", [1, ST])

        z_ps = ps("z_ps", [128, 3, COLS])
        sel_ps = ps("sel_ps", [128, 2, 2, COLS])
        top_ps = ps("top_ps", [128, COLS])

        s_index = sem("index_loaded")
        s_const = sem("consts_loaded")
        s_w0 = sem("w0_loaded")
        s_wstage = sem("split_weights_loaded")
        s_wwhole = sem("whole_weights_loaded")
        s_top = sem("top_weights_loaded")
        s_bias = sem("biases_loaded")
        s_dense = sem("dense_loaded")
        s_stored = sem("y_stored")
        s_gathered = sem("rows_gathered")
        s_part = sem("parts_ready")
        s_rest = sem("rests_ready")
        s_transposed = sem("parts_transposed")
        s_stacked = sem("stacked_ready")
        s_op_made = sem("pair_ops_selected")
        s_op_ready = sem("pair_ops_ready")
        s_bc_made = sem("x0_rows_selected")
        s_bc_ready = sem("x0_rows_ready")
        s_prod = {la: sem(f"products{la}_ready") for la in (0, 1, 2)}
        s_high = {la: sem(f"high{la}_ready") for la in (1, 2)}
        s_low = {la: sem(f"low{la}_ready") for la in (1, 2)}
        s_mm = {la: sem(f"group{la}_contracted") for la in (0, 1, 2)}
        s_z = {la: sem(f"z{la}_taken") for la in (0, 1, 2)}
        s_wprep = sem("weights_prepared")
        s_sum = sem("sum_steps")
        s_h1 = sem("hidden1_contracted")
        s_h1r = sem("hidden1_ready")
        s_h2 = sem("hidden2_contracted")
        s_h2r = sem("hidden2_ready")
        s_y = sem("y_contracted")
        s_yr = sem("y_ready")

        def count(per_tile, u, k, more):
            return u * (CT * per_tile) + (per_tile * k + more)

        def number(u):
            return isinstance(u, int)

        def wait(eng, s, value):
            if not isinstance(value, int) or value > 0:
                eng.wait_ge(s, value)

        n_prep = 2 + 4

        block = ctx.enter_context(nc.Block())

        @block.sync
        def _(sp):
            ids_v = ids.rearrange("(t p) f -> t p f", p=ST)
            dense_v = dense.rearrange("c (t p) -> t c p", p=ST)
            out_v = out.rearrange("(t p) one -> t one p", p=ST)

            def load_index(t):
                sp.dma_start(index_sb[:, :], ids_v[t, :, :]).then_inc(s_index, 16)

            load_index(0)
            sp.dma_start(identity_sb[:, :], identity).then_inc(s_const, 16)
            sp.dma_start(select_sb[:, :, :], select).then_inc(s_const, 16)
            full = PAIR_CHUNKS - 1
            sp.dma_start(w0_sb[:, 0:full, :], w0_fwd[0:full * PAIR_ROWS, :].rearrange("(c p) s -> p c s", p=PAIR_ROWS)).then_inc(s_w0, 16)
            sp.dma_start(w0_sb[0:PAIR_TAIL, full, :], w0_fwd[full * PAIR_ROWS:, :]).then_inc(s_w0, 16)
            rev = products[:, 0, :, :].rearrange("p g c -> p (g c)").rearrange("p (c s) -> p c s", s=SIZE)
            sp.dma_start(rev[0:PAIR_ROWS, 0:full, :], w0_rev[0:full * PAIR_ROWS, :].rearrange("(c p) s -> p c s", p=PAIR_ROWS)).then_inc(s_w0, 16)
            sp.dma_start(rev[0:FIELDS, full, :], w0_rev[full * PAIR_ROWS:, :]).then_inc(s_w0, 16)
            sp.dma_start(columns_sb[:, :], columns).then_inc(s_bias, 16)
            for n, (layer, w) in enumerate(((1, w1), (2, w2))):
                rows = 128 * GROUP
                stage = products[:, 1 + n, :, :].rearrange("p g c -> p (g c)").rearrange("p (c s) -> p c s", s=SIZE)
                for i, g in enumerate(SPLIT):
                    sp.dma_start(stage[:, i * GROUP:(i + 1) * GROUP, :],
                                 w[g * rows:(g + 1) * rows, :].rearrange("(c p) s -> p c s", p=128)).then_inc(s_wstage, 16)
                for i, g in enumerate(WHOLE):
                    have = GROUP if g < GROUPS - 1 else GROUP - 1
                    sp.dma_start(w_whole[layer][:, i * GROUP:i * GROUP + have, :],
                                 w[g * rows:g * rows + 128 * have, :].rearrange("(c p) s -> p c s", p=128)).then_inc(s_wwhole, 16)
                sp.dma_start(w_whole[layer][0:TAIL, len(WHOLE) * GROUP - 1, :], w[128 * (CHUNKS - 1):, :]).then_inc(s_wwhole, 16)
            sp.wait_ge(s_gathered, 16 * FIELDS)
            load_index(1)
            sp.dma_start(top1_sb[0:HALF, 0, :], w_top1[HALF:SIZE, :]).then_inc(s_top, 16)
            sp.dma_start(top1_sb[HALF:SIZE, 0, :], w_top1[0:HALF, :]).then_inc(s_top, 16)
            sp.dma_start(top1_sb[:, 1, :], w_top1[SIZE:2 * SIZE, :]).then_inc(s_top, 16)
            sp.dma_start(top1_dense_sb[:, :], w_top1[2 * SIZE:, :]).then_inc(s_top, 16)
            sp.dma_start(top2_sb[:, :, :], w_top2.rearrange("(m p) n -> p m n", p=128)).then_inc(s_top, 16)

            def mlp_io(t, before):
                if before:
                    sp.wait_ge(s_h1, before)
                sp.dma_start(dense_sb[:, :], dense_v[t, :, :]).then_inc(s_dense, 16)
                sp.wait_ge(s_yr, t + 1)
                sp.dma_start(out_v[t, :, :], y_sb[:, :]).then_inc(s_stored, 16)

            with sp.Fori(0, SAMPLE_TILES - 1) as u:
                sp.wait_ge(s_gathered, (u + 2) * (16 * FIELDS))
                load_index(u + 2)
                sp.dma_start(dense_sb[:, :], dense_v[u, :, :]).then_inc(s_dense, 16)
                sp.wait_ge(s_yr, u + 1)
                sp.dma_start(out_v[u, :, :], y_sb[:, :]).then_inc(s_stored, 16)
            mlp_io(SAMPLE_TILES - 1, 0)
            sp.wait_ge(s_stored, 16 * SAMPLE_TILES)

        @block.gpsimd
        def _(pool):
            def gather(fields):
                for f in fields:
                    nc.gpsimd.indirect_dma_start(
                        out=rows_sb[:, f, :], out_offset=None, in_=tables[f],
                        in_offset=bass.IndirectOffsetOnAxis(ap=index_sb[:, f:f + 1], axis=0),
                    ).then_inc(s_gathered, 16)

            def rests(t):
                pool.wait_ge(s_part, t * PARTS + 1)
                nc.gpsimd.tensor_tensor(rest_sb[:, :, :], rows_sb[:, :, :].rearrange("p f d -> p d f"),
                                        parts_sb[:, :, 0, :], ALU.subtract).then_inc(s_rest, 1)
                pool.wait_ge(s_part, t * PARTS + 2)
                nc.gpsimd.tensor_tensor(rest_sb[:, :, :], rest_sb[:, :, :], parts_sb[:, :, 1, :], ALU.subtract).then_inc(s_rest, 1)

            def sums(u, k):
                q = k % CT
                for n, direct in enumerate((direct01, direct2)):
                    if n == 0:
                        pool.wait_ge(s_z[0], count(3, u, k, 3))
                        pool.wait_ge(s_z[1], count(3, u, k, 3))
                    else:
                        pool.wait_ge(s_z[2], count(1, u, k, 1))
                    src = direct[:, k % 2, :]
                    half, whole, run = half_sum[:, n, :], tile_sum[:, n, :], running[:, n, :]
                    nc.gpsimd.tensor_tensor(half, src[:, 0:COLS // 2], src[:, COLS // 2:COLS], ALU.add).then_inc(s_sum, 1)
                    pool.wait_ge(s_sum, count(6, u, k, 3 * n + 1))
                    if q == 0:
                        nc.gpsimd.tensor_tensor(run, half[:, 0:ST], half[:, ST:2 * ST], ALU.add).then_inc(s_sum, 2)
                        continue
                    nc.gpsimd.tensor_tensor(whole, half[:, 0:ST], half[:, ST:2 * ST], ALU.add).then_inc(s_sum, 1)
                    pool.wait_ge(s_sum, count(6, u, k, 3 * n + 2))
                    if q < CT - 1:
                        nc.gpsimd.tensor_tensor(run, run, whole, ALU.add).then_inc(s_sum, 1)
                    else:
                        if n == 0:
                            wait(pool, s_h1, u + (k // CT))
                        nc.gpsimd.tensor_tensor(features[:, n, :], run, whole, ALU.add).then_inc(s_sum, 1)

            pool.wait_ge(s_index, 16)
            gather(range(FIELDS))
            rests(0)
            pool.wait_ge(s_index, 2 * 16)
            gather(range(FIELDS))
            with pool.Fori(0, SAMPLE_TILES - 1) as u:
                for q in range(CT):
                    sums(u, q)
                    if q == 0:
                        rests(u + 1)
                        pool.wait_ge(s_index, (u + 3) * 16)
                    else:
                        gather(range((q - 1) * GATHERS, q * GATHERS))
            for k in range(COLUMN_TILES - CT, COLUMN_TILES):
                sums(0, k)
            pool.wait_ge(s_gathered, 16 * FIELDS * (SAMPLE_TILES + 1))

        @block.tensor
        def _(pe):
            def transposes(t, u, k):
                pe.wait_ge(s_part, t * PARTS + PARTS)
                for h in range(2):
                    if k is not None:
                        pe.wait_ge(s_bc_ready, count(BC_ITEMS, u, k, BC_ITEMS - 1 + h))
                    dst = sel_ps[:, h, 0, :].bitcast(bf16)
                    for d in range(DIM // 2):
                        last = nc.tensor.transpose(
                            dst[0:STACK, d * ST:(d + 1) * ST],
                            parts_sb[:, h * (DIM // 2) + d, :, :].rearrange("p s f -> p (s f)"), identity_sb[:, :])
                    last.then_inc(s_transposed, 1)

            def select_two(item, k, first):
                for n in range(2):
                    last = nc.tensor.matmul(sel_ps[:, item % 2, n, :], select_sb[:, first + 2 * item + n, :],
                                            stacked[:, k % CT, :], start=True, stop=True)
                return last

            def select_ops(u, k, i):
                if i >= 2:
                    pe.wait_ge(s_op_ready, count(OP_ITEMS, u, k, i - 1))
                elif k % CT == 0:
                    pe.wait_ge(s_stacked, u * 2 + (k // CT) * 2 + 2)
                else:
                    pe.wait_ge(s_bc_ready, count(BC_ITEMS, u, k - 1, BC_ITEMS - 1 + i))
                select_two(i, k, 0).then_inc(s_op_made, 1)

            def select_rows(u, k, i):
                if i >= 2:
                    pe.wait_ge(s_bc_ready, count(BC_ITEMS, u, k, i - 1))
                else:
                    pe.wait_ge(s_op_ready, count(OP_ITEMS, u, k, OP_ITEMS - 1 + i))
                select_two(i, k, OPERANDS).then_inc(s_bc_made, 1)

            def contract(u, k, s):
                layer, g = SLOTS[s]
                k += ahead(layer)
                z = z_ps[:, layer, :]
                buffer = s % RING
                if g == 0:
                    wait(pe, s_z[layer], count({0: 3, 1: 3, 2: 1}[layer], u, k, 0))
                if layer == 0:
                    pe.wait_ge(s_prod[0], count(PER_TILE[0], u, k, g + 1))
                    a, b = PAIR_GROUPS[g]
                    for c in range(a, b):
                        rows = PAIR_ROWS if c < PAIR_CHUNKS - 1 else PAIR_TAIL
                        last = nc.tensor.matmul(z, w0_sb[0:rows, c, :], products[0:rows, buffer, c - a, :],
                                                start=(c == 0), stop=(c == PAIR_CHUNKS - 1))
                elif g in WHOLE:
                    pe.wait_ge(s_prod[layer], count(GROUPS, u, k, g + 1))
                    for n in range(GROUP):
                        c = GROUP * g + n
                        rows = 128 if c < CHUNKS - 1 else TAIL
                        last = nc.tensor.matmul(z, w_whole[layer][0:rows, WHOLE.index(g) * GROUP + n, :],
                                                products[0:rows, buffer, n, :],
                                                start=(c == 0), stop=(c == CHUNKS - 1))
                else:
                    i = SPLIT.index(g)
                    ring = SPLIT_SLOTS.index(s) % SPLIT_RING
                    pe.wait_ge(s_high[layer], count(NSPLIT, u, k, i + 1))
                    for n in range(GROUP):
                        c = i * GROUP + n
                        first = g == 0 and n == 0
                        nc.tensor.matmul(z, w_high[layer][:, c, :], prod_high[:, ring, n, :], start=first, stop=False)
                        nc.tensor.matmul(z, w_low[layer][:, c, :], prod_high[:, ring, n, :], start=False, stop=False)
                    pe.wait_ge(s_low[layer], count(NSPLIT, u, k, i + 1))
                    for n in range(GROUP):
                        c = i * GROUP + n
                        last = nc.tensor.matmul(z, w_high[layer][:, c, :], prod_low[:, ring, n, :],
                                                start=False, stop=(g == GROUPS - 1 and n == GROUP - 1))
                last.then_inc(s_mm[layer], 1)

            def mlp1(t):
                pe.wait_ge(s_sum, t * (6 * CT) + 6 * CT)
                pe.wait_ge(s_dense, t * 16 + 16)
                wait(pe, s_yr, t)
                for m in range(HID1 // 128):
                    cols = slice(m * 128, (m + 1) * 128)
                    nc.tensor.matmul(top_ps[:, cols], top1_sb[:, 0, cols], features[:, 0, :], start=True, stop=False)
                    nc.tensor.matmul(top_ps[:, cols], top1_sb[:, 1, cols], features[:, 1, :], start=False, stop=False)
                    last = nc.tensor.matmul(top_ps[:, cols], top1_dense_sb[:, cols], dense_sb[:, :], start=False, stop=True)
                last.then_inc(s_h1, 1)

            def mlp2(t):
                pe.wait_ge(s_h1r, t * (HID1 // 128) + HID1 // 128)
                for m in range(HID2 // 128):
                    cols = slice(m * 128, (m + 1) * 128)
                    for c in range(HID1 // 128):
                        last = nc.tensor.matmul(top_ps[:, cols], top2_sb[:, c, cols], hidden1[:, c, :],
                                                start=(c == 0), stop=(c == HID1 // 128 - 1))
                last.then_inc(s_h2, 1)

            def mlp3(t):
                pe.wait_ge(s_h2r, t * (HID2 // 128) + HID2 // 128)
                for c in range(HID2 // 128):
                    last = nc.tensor.matmul(top_ps[0:1, 0:ST], top3_sb[:, c:c + 1], hidden2[:, c, :],
                                            start=(c == 0), stop=(c == HID2 // 128 - 1))
                last.then_inc(s_y, 1)

            def period(u, k, has_next=True, transpose=None, mlp=None):
                for s, (layer, g) in enumerate(SLOTS):
                    if layer != 0 or has_next:
                        contract(u, k, s)
                    if has_next and s < 2:
                        select_ops(u, k + 1, 2 * s)
                        select_ops(u, k + 1, 2 * s + 1)
                    if has_next and layer == 2:
                        select_rows(u, k + 1, 2 * g)
                        select_rows(u, k + 1, 2 * g + 1)
                    if mlp is not None and s == END0:
                        mlp1(mlp)
                    if mlp is not None and s == END0 + 2:
                        mlp2(mlp)
                    if mlp is not None and s == END0 + 4:
                        mlp3(mlp)
                if transpose is not None:
                    transposes(transpose, u, k + 1)

            pe.wait_ge(s_const, 2 * 16)
            transposes(0, 0, None)
            for i in range(OP_ITEMS):
                select_ops(0, 0, i)
            for i in range(4):
                select_rows(0, 0, i)
            pe.wait_ge(s_wprep, 2)
            contract(0, -1, END1 + 1)
            select_rows(0, 0, 4)
            select_rows(0, 0, 5)
            contract(0, -1, END0)
            for i in range(6, BC_ITEMS):
                select_rows(0, 0, i)
            pe.wait_ge(s_wprep, n_prep)
            pe.wait_ge(s_wwhole, 2 * (len(WHOLE) + 1) * 16)
            period(0, 0)
            pe.wait_ge(s_top, 5 * 16)
            with pe.Fori(0, SAMPLE_TILES - 1) as u:
                for q in range(CT):
                    period(u, q + 1, transpose=u + 1 if q == 1 else None, mlp=u if q == CT - 1 else None)
            for k in range(COLUMN_TILES - CT + 1, COLUMN_TILES):
                period(0, k, has_next=k < COLUMN_TILES - 1)
            mlp1(SAMPLE_TILES - 1)
            mlp2(SAMPLE_TILES - 1)
            mlp3(SAMPLE_TILES - 1)

        @block.vector
        def _(dve):
            def product(u, k, s):
                layer, g = SLOTS[s]
                before = user_before(k, s, number(u))
                if before is not None:
                    off, slot = before
                    la, gb = SLOTS[slot]
                    if la == 0 or gb in WHOLE:
                        dve.wait_ge(s_mm[la], count(PER_TILE[la], u, k + off + ahead(la), gb + 1))
                    else:
                        dve.wait_ge(s_low[la], count(NSPLIT, u, k + off, SPLIT.index(gb) + 1))
                k += ahead(layer)
                buffer = s % RING
                if layer == 0:
                    a, b = PAIR_GROUPS[g]
                    dve.wait_ge(s_op_ready, count(OP_ITEMS, u, k, (b + 2) // 2))
                    n = b - a
                    left = pair_ops[:, 0:1, :].broadcast_to([128, n, COLS])
                    right = pair_ops[:, 1 + a:1 + b, :]
                else:
                    if layer == 1:
                        dve.wait_ge(s_bc_ready, count(BC_ITEMS, u, k, 2 * g + 2))
                    if g == 0:
                        dve.wait_ge(s_z[layer - 1], count(3, u, k, 2))
                    n = GROUP
                    xk = (x1_rows if layer == 1 else x2_rows)
                    left = x0_rows[:, GROUP * g:GROUP * (g + 1), :]
                    right = xk[:, None, :].broadcast_to([128, n, COLS])
                nc.vector.tensor_tensor(products[:, buffer, 0:n, :], left, right, ALU.mult).then_inc(s_prod[layer], 1)

            def low(u, k, s):
                layer, g = SLOTS[s]
                ring = SPLIT_SLOTS.index(s) % SPLIT_RING
                dve.wait_ge(s_high[layer], count(NSPLIT, u, k, SPLIT.index(g) + 1))
                nc.vector.tensor_tensor(prod_low[:, ring, :, :], products[:, s % RING, :, :],
                                        prod_high[:, ring, :, :].bitcast(f32), ALU.subtract).then_inc(s_low[layer], 1)

            def period(u, k, has_next=True):
                for s, (layer, g) in enumerate(SLOTS):
                    if layer != 0 or has_next:
                        product(u, k, s)
                    if s - 1 in SPLIT_SLOTS:
                        low(u, k, s - 1)

            full = PAIR_CHUNKS - 1
            rev = products[:, 0, :, :].rearrange("p g c -> p (g c)").rearrange("p (c s) -> p c s", s=SIZE)
            dve.wait_ge(s_w0, 4 * 16)
            nc.vector.tensor_tensor(w0_sb[:, 0:full, :], w0_sb[:, 0:full, :], rev[0:PAIR_ROWS, 0:full, :], ALU.add).then_inc(s_wprep, 1)
            nc.vector.tensor_tensor(w0_sb[0:FIELDS, full, :], w0_sb[0:FIELDS, full, :], rev[0:FIELDS, full, :], ALU.add).then_inc(s_wprep, 1)
            dve.wait_ge(s_wstage, 2 * NSPLIT * 16)
            for n, layer in enumerate((1, 2)):
                stage = products[:, 1 + n, :, :].rearrange("p g c -> p (g c)").rearrange("p (c s) -> p c s", s=SIZE)[:, 0:NSPLIT * GROUP, :]
                nc.vector.tensor_copy(w_high[layer][:, :, :], stage).then_inc(s_wprep, 1)
                dve.wait_ge(s_wprep, 2 + 2 * n + 1)
                nc.vector.tensor_tensor(w_low[layer][:, :, :], stage, w_high[layer][:, :, :].bitcast(f32), ALU.subtract).then_inc(s_wprep, 1)
            dve.wait_ge(s_wprep, n_prep)
            product(0, -1, END1 + 1)
            product(0, -1, END0)
            period(0, 0)
            with dve.Fori(0, SAMPLE_TILES - 1) as u:
                for q in range(CT):
                    period(u, q + 1)
            for k in range(COLUMN_TILES - CT + 1, COLUMN_TILES):
                period(0, k, has_next=k < COLUMN_TILES - 1)

        @block.scalar
        def _(act):
            def part(t, n):
                if n == 0:
                    act.wait_ge(s_gathered, (t + 1) * (16 * FIELDS))
                    wait(act, s_transposed, t * 2)
                    src = rows_sb[:, :, :].rearrange("p f d -> p d f")
                else:
                    act.wait_ge(s_rest, t * (PARTS - 1) + n)
                    src = rest_sb[:, :, :]
                nc.scalar.activation(parts_sb[:, :, n, :], src, ACT.Copy).then_inc(s_part, 1)

            def take_transposed(t):
                for h in range(2):
                    act.wait_ge(s_transposed, t * 2 + h + 1)
                    nc.scalar.activation(stacked[:, 2 * h:2 * h + 2, :].rearrange("p q c -> p (q c)"),
                                         sel_ps[:, h, 0, :].bitcast(bf16)[0:STACK, :], ACT.Copy).then_inc(s_stacked, 1)

            def take_ops(u, k, i):
                act.wait_ge(s_op_made, count(OP_ITEMS, u, k, i + 1))
                if i == 0:
                    wait(act, s_prod[0], count(PER_TILE[0], u, k, 0))
                nc.scalar.activation(pair_ops[:, 2 * i:2 * i + 2, :], sel_ps[:, i % 2, :, :], ACT.Copy).then_inc(s_op_ready, 1)

            def take_rows(u, k, i):
                act.wait_ge(s_bc_made, count(BC_ITEMS, u, k, i + 1))
                if i % 2 == 0:
                    wait(act, s_prod[2], count(GROUPS, u, k - 1, i // 2 + 1))
                nc.scalar.activation(x0_rows[:, 2 * i:2 * i + 2, :], sel_ps[:, i % 2, :, :], ACT.Copy).then_inc(s_bc_ready, 1)

            def high(u, k, s):
                layer, g = SLOTS[s]
                i = SPLIT_SLOTS.index(s)
                before = split_before(k, i, number(u))
                if before is not None:
                    off, slot = before
                    la, gb = SLOTS[slot]
                    act.wait_ge(s_mm[la], count(GROUPS, u, k + off, gb + 1))
                act.wait_ge(s_prod[layer], count(GROUPS, u, k, g + 1))
                nc.scalar.activation(prod_high[:, i % SPLIT_RING, :, :], products[:, s % RING, :, :], ACT.Copy).then_inc(s_high[layer], 1)

            def relu(dst, src, bias, done):
                nc.scalar.activation(dst, src, ACT.Relu, bias=bias).then_inc(done, 1)

            def take_z(u, k, layer):
                act.wait_ge(s_mm[layer], count(PER_TILE[layer], u, k, PER_TILE[layer]))
                z, bias = z_ps[:, layer, :], bias_sb[:, layer:layer + 1]
                summed = k - 2 if number(u) or k >= 2 else k - 1
                if layer < 2:
                    xk = x1_rows if layer == 0 else x2_rows
                    wait(act, s_prod[layer + 1], count(GROUPS, u, k - 1, GROUPS))
                    relu(xk[0:HALF, :], z[0:HALF, :], bias[0:HALF, :], s_z[layer])
                    relu(xk[HALF:SIZE, :], z[0:HALF, :], bias[0:HALF, :], s_z[layer])
                    dst = direct01[HALF:SIZE, k % 2, :] if layer == 0 else direct01[0:HALF, k % 2, :]
                    wait(act, s_sum, count(6, u, summed, 1))
                    relu(dst, z[HALF:SIZE, :], bias[HALF:SIZE, :], s_z[layer])
                else:
                    wait(act, s_sum, count(6, u, summed, 4))
                    relu(direct2[:, k % 2, :], z, bias, s_z[2])

            def mlp_relu1(t):
                act.wait_ge(s_h1, t + 1)
                for m in range(HID1 // 128):
                    relu(hidden1[:, m, :], top_ps[:, m * 128:(m + 1) * 128], bias_top1_sb[:, m:m + 1], s_h1r)

            def mlp_relu2(t):
                act.wait_ge(s_h2, t + 1)
                for m in range(HID2 // 128):
                    relu(hidden2[:, m, :], top_ps[:, m * 128:(m + 1) * 128], bias_top2_sb[:, m:m + 1], s_h2r)

            def mlp_out(t):
                act.wait_ge(s_y, t + 1)
                wait(act, s_stored, t * 16)
                nc.scalar.activation(y_sb[:, :], top_ps[0:1, 0:ST], ACT.Copy).then_inc(s_yr, 1)

            def period(u, k, has_next=True, parts=None, transpose=None, mlp=None):
                for s, (layer, g) in enumerate(SLOTS):
                    if s + 2 in SPLIT_SLOTS:
                        high(u, k, s + 2)
                    elif has_next and s + 2 - len(SLOTS) in SPLIT_SLOTS:
                        high(u, k + 1, s + 2 - len(SLOTS))
                    if s == END1:
                        take_z(u, k, 1)
                    if s == END0 and has_next:
                        take_z(u, k + 1, 0)
                    if s == END2:
                        take_z(u, k, 2)
                    if has_next and s < 2:
                        take_ops(u, k + 1, 2 * s)
                        take_ops(u, k + 1, 2 * s + 1)
                    if has_next and layer == 2:
                        take_rows(u, k + 1, 2 * g)
                        take_rows(u, k + 1, 2 * g + 1)
                    if parts is not None and s in PART_STEPS:
                        part(parts, PART_STEPS.index(s))
                    if mlp is not None and s == END0 + 1:
                        mlp_relu1(mlp)
                    if mlp is not None and s == END0 + 3:
                        mlp_relu2(mlp)
                    if mlp is not None and s == END0 + 5:
                        mlp_out(mlp)
                if transpose is not None:
                    take_transposed(transpose)

            act.wait_ge(s_bias, 16)
            for n in range(PARTS):
                part(0, n)
            take_transposed(0)
            for i in range(OP_ITEMS):
                take_ops(0, 0, i)
            for i in range(6):
                take_rows(0, 0, i)
            take_z(0, 0, 0)
            for i in range(6, BC_ITEMS):
                take_rows(0, 0, i)
            for s in range(2):
                if s in SPLIT_SLOTS:
                    high(0, 0, s)
            period(0, 0)
            with act.Fori(0, SAMPLE_TILES - 1) as u:
                for q in range(CT):
                    period(u, q + 1, parts=u + 1 if q == 0 else None, transpose=u + 1 if q == 1 else None, mlp=u if q == CT - 1 else None)
            for k in range(COLUMN_TILES - CT + 1, COLUMN_TILES):
                period(0, k, has_next=k < COLUMN_TILES - 1)
            mlp_relu1(SAMPLE_TILES - 1)
            mlp_relu2(SAMPLE_TILES - 1)
            mlp_out(SAMPLE_TILES - 1)


def pair_order():
    h = np.tile(np.arange(FIELDS), DISTANCES + 1)
    j = np.repeat(np.append(np.arange(1, DISTANCES + 1), 0), FIELDS)
    return h, (h + j) % FIELDS


def selection():
    _, right = pair_order()
    want = np.full((OPERANDS + CHUNKS, 128), -1)
    want[0, :PAIR_ROWS] = np.tile(np.arange(FIELDS), PAIR_BLOCKS)
    for c in range(PAIR_CHUNKS):
        rows = right[c * PAIR_ROWS:(c + 1) * PAIR_ROWS]
        want[1 + c, :len(rows)] = rows
    want[OPERANDS:] = np.minimum(np.arange(CHUNKS * 128) // HALF, FIELDS - 1).reshape(CHUNKS, 128)
    return (np.arange(STACK)[:, None, None] % FIELDS == want[None]).astype(np.float32)


def kernel(**inputs):
    import ml_dtypes
    import concourse.bacc as bacc
    from concourse.bass_utils import run_bass_kernel_spmd

    a = {name: np.ascontiguousarray(x) for name, x in inputs.items()}
    left, right = pair_order()
    w0 = a["L0_rec_w0"]
    arrays = {
        "dense": np.ascontiguousarray(a["dense_ctx"].T),
        "ids": np.concatenate([a["ids"], np.zeros((ST, FIELDS), a["ids"].dtype)]),
        "w0_fwd": w0[left, right],
        "w0_rev": w0[right, left][:DISTANCES * FIELDS],
        "w1": a["L0_rec_w1"].reshape(ROWS, SIZE),
        "w2": a["L0_rec_w2"].reshape(ROWS, SIZE),
        "w_top1": a["W_top1"], "w_top2": a["W_top2"],
        "columns": np.concatenate([a[n].reshape(-1, 128) for n in ("L0_rec_b0", "L0_rec_b1", "L0_rec_b2", "b_top1", "b_top2", "W_top3")]).T,
        "select": selection().astype(ml_dtypes.bfloat16),
        "identity": np.eye(128, dtype=ml_dtypes.bfloat16),
    }
    for f in range(FIELDS):
        arrays[f"tbl_{f}"] = a[f"tbl_{f}"]
    arrays = {f"in_{name}": np.ascontiguousarray(x) for name, x in arrays.items()}

    nc = bacc.Bacc("TRN2", target_bir_lowering=False, num_devices=1)
    ap = {name[3:]: nc.dram_tensor(name, x.shape, mybir.dt.from_np(x.dtype), kind="ExternalInput").ap()
          for name, x in arrays.items()}
    out = nc.dram_tensor("out_y", (BATCH, 1), mybir.dt.float32, kind="ExternalOutput").ap()
    build(nc, tables=[ap.pop(f"tbl_{f}") for f in range(FIELDS)], out=out, **ap)
    r = run_bass_kernel_spmd(nc, [arrays], core_ids=[0])
    return r.results[0]["out_y"]
```

```python
from contextlib import ExitStack

import numpy as np

import concourse.bass as bass
from concourse import mybir

BATCH, FIELDS, DIM, DENSE = 1024, 39, 16, 16
SIZE = 128
HALF = SIZE // 2
HID1, HID2 = 512, 256
ST = 128
SAMPLE_TILES = BATCH // ST
COLS = 512
CT = ST * DIM // COLS
COLUMN_TILES = SAMPLE_TILES * CT
PARTS = 3
STACK = PARTS * FIELDS
DISTANCES = (FIELDS - 1) // 2
PAIR_BLOCKS = 3
PAIR_ROWS = PAIR_BLOCKS * FIELDS
PAIR_CHUNKS = -(-(DISTANCES + 1) // PAIR_BLOCKS)
PAIR_TAIL = (DISTANCES + 1 - PAIR_BLOCKS * (PAIR_CHUNKS - 1)) * FIELDS
ROWS = FIELDS * HALF
CHUNKS = -(-ROWS // 128)
TAIL = ROWS - 128 * (CHUNKS - 1)
GROUP = 4
GROUPS = CHUNKS // GROUP
SPLIT = {1: (2, 3, 4), 2: (1, 2, 3)}
WHOLE = {la: tuple(g for g in range(GROUPS) if g not in SPLIT[la]) for la in (1, 2)}
PAIR_GROUPS = ((0, 4), (4, PAIR_CHUNKS))
BC_ITEMS = CHUNKS // 2
RING = 4
SPLIT_RING = 2
WORK = [(la, g) for la in (1, 2) for g in range(GROUPS)]
SPLIT_WORK = [x for x in WORK if x[1] in SPLIT[x[0]]]
PER_TILE = {0: len(PAIR_GROUPS), 1: GROUPS, 2: GROUPS}
GATHERS = FIELDS // (CT - 1)
assert CT * len(WORK) % RING == 0 and CT * len(SPLIT_WORK) % SPLIT_RING == 0


def buffer_of(work, ring, k, what):
    return (len(work) * k + work.index(what)) % ring


def user_before(work, ring, k, what):
    tile, n = divmod(len(work) * k + work.index(what) - ring, len(work))
    return tile, work[n]


def selections():
    out = [("parts", 0, 0), ("parts", 0, 1)]
    for j in range(-2, COLUMN_TILES):
        here = [("left", j + 2, 0)] + [("rows", j + 1, i) for i in range(BC_ITEMS)]
        out += [x for x in here if 0 <= x[1] < COLUMN_TILES]
        if j > 0 and j % 2 and j // CT + 1 < SAMPLE_TILES:
            out.append(("parts", j // CT + 1, j % CT // 2))
    return out


SELECTIONS = selections()


def build(nc, dense, ids, tables, w0_fwd, w0_rev, w1, w2, w_top1, w_top2, columns, select, identity, out):
    f32, f32r, bf16, i32 = mybir.dt.float32, mybir.dt.float32r, mybir.dt.bfloat16, mybir.dt.int32
    ACT, ALU = mybir.ActivationFunctionType, mybir.AluOpType

    with ExitStack() as ctx:
        def sb(name, shape, dt=f32):
            return ctx.enter_context(nc.sbuf_tensor(name, shape, dt))

        def ps(name, shape):
            return ctx.enter_context(nc.psum_tensor(name, shape, f32))

        def sem(name):
            return ctx.enter_context(nc.semaphore(name))

        select_sb = sb("select_sb", [STACK, 1 + CHUNKS, 128], bf16)
        identity_sb = sb("identity_sb", [128, 128], bf16)
        w0_sb = sb("w0_sb", [PAIR_ROWS, PAIR_CHUNKS, SIZE])
        w_whole = {la: sb(f"w{la}_whole", [128, len(WHOLE[la]) * GROUP, SIZE]) for la in (1, 2)}
        w_high = {la: sb(f"w{la}_high", [128, len(SPLIT[la]) * GROUP, SIZE], f32r) for la in (1, 2)}
        w_low = {la: sb(f"w{la}_low", [128, len(SPLIT[la]) * GROUP, SIZE], f32r) for la in (1, 2)}
        columns_sb = sb("columns_sb", [128, 3 + HID1 // 128 + 2 * (HID2 // 128)])
        bias_sb = columns_sb[:, 0:3]
        bias_top1_sb = columns_sb[:, 3:3 + HID1 // 128]
        bias_top2_sb = columns_sb[:, 3 + HID1 // 128:3 + HID1 // 128 + HID2 // 128]
        top3_sb = columns_sb[:, 3 + HID1 // 128 + HID2 // 128:]
        top1_sb = sb("top1_sb", [128, 2, HID1])
        top1_dense_sb = sb("top1_dense_sb", [DENSE, HID1])
        top2_sb = sb("top2_sb", [128, HID1 // 128, HID2])
        index_sb = sb("index_sb", [ST, FIELDS], i32)
        rows_sb = sb("rows_sb", [ST, FIELDS, DIM])
        rest_sb = sb("rest_sb", [ST, DIM, FIELDS])
        parts_sb = sb("parts_sb", [ST, DIM, PARTS, FIELDS], bf16)
        stacked = sb("stacked", [STACK, CT, COLS], bf16)
        pair_ops = sb("pair_ops", [128, 1 + PAIR_CHUNKS, COLS])
        x0_rows = sb("x0_rows", [128, CHUNKS, COLS])
        products = sb("products", [128, RING, GROUP, COLS])
        prod_high = sb("prod_high", [128, SPLIT_RING, GROUP, COLS], f32r)
        prod_low = sb("prod_low", [128, SPLIT_RING, GROUP, COLS], f32r)
        direct01 = sb("direct01", [128, 2, COLS])
        direct2 = sb("direct2", [128, 2, COLS])
        running = sb("running", [128, 2, ST])
        features = sb("features", [128, 2, ST])
        dense_sb = sb("dense_sb", [DENSE, ST])
        hidden1 = sb("hidden1", [128, HID1 // 128, ST])
        hidden2 = sb("hidden2", [128, HID2 // 128, ST])
        y_sb = sb("y_sb", [1, BATCH])

        z_ps = ps("z_ps", [128, 3, COLS])
        sel_ps = ps("sel_ps", [128, 2, 2, COLS])
        top_ps = ps("top_ps", [128, COLS])

        s_index = sem("index_loaded")
        s_const = sem("consts_loaded")
        s_w0 = sem("w0_loaded")
        s_wstage = sem("split_weights_loaded")
        s_wwhole = sem("whole_weights_loaded")
        s_top = sem("top_weights_loaded")
        s_bias = sem("biases_loaded")
        s_dense = sem("dense_loaded")
        s_stored = sem("y_stored")
        s_gathered = sem("rows_gathered")
        s_part = sem("parts_ready")
        s_rest = sem("rests_ready")
        s_transposed = sem("parts_transposed")
        s_stacked = sem("stacked_ready")
        s_left_made = sem("left_side_selected")
        s_left = sem("left_side_ready")
        s_bc_made = sem("x0_rows_selected")
        s_bc_ready = sem("x0_rows_ready")
        s_blank = sem("unused_rows_cleared")
        s_right = [sem(f"right_sides{g}_copied") for g in range(len(PAIR_GROUPS))]
        s_prod = {la: sem(f"products{la}_ready") for la in (0, 1, 2)}
        s_high = {la: sem(f"high{la}_ready") for la in (1, 2)}
        s_low = {la: sem(f"low{la}_ready") for la in (1, 2)}
        s_used = {la: sem(f"high{la}_used") for la in (1, 2)}
        s_mm = {la: sem(f"group{la}_contracted") for la in (0, 1, 2)}
        s_z = {la: sem(f"z{la}_taken") for la in (0, 1, 2)}
        s_wprep = sem("weights_prepared")
        s_sum = sem("sum_steps")
        s_h1 = sem("hidden1_contracted")
        s_h1r = sem("hidden1_ready")
        s_h2 = sem("hidden2_contracted")
        s_h2r = sem("hidden2_ready")
        s_y = sem("y_contracted")
        s_yr = sem("y_ready")

        def count(per_tile, u, k, more):
            return u * (CT * per_tile) + (per_tile * k + more)

        def number(u):
            return isinstance(u, int)

        def real(u, k):
            return not number(u) or 0 <= CT * u + k < COLUMN_TILES

        def selection_buffer(kind, u, k, i):
            per = 1 if kind == "parts" else CT
            at = 0 if number(u) else 1
            n = SELECTIONS.index((kind, per * at + k, i))
            if n < 2:
                return n % 2, None, 0
            before, tile, item = SELECTIONS[n - 2]
            if before == "parts":
                return n % 2, s_stacked, u * 2 + (2 * (tile - at) + item + 1)
            tile -= CT * at
            if before == "left":
                return n % 2, s_left, count(1, u, tile, 1)
            return n % 2, s_bc_ready, count(BC_ITEMS, u, tile, item + 1)

        def wait(eng, s, value):
            if not isinstance(value, int) or value > 0:
                eng.wait_ge(s, value)

        n_prep = 2 + 4
        n_stage = sum(len(SPLIT[la]) + 2 * (GROUPS - 1 in SPLIT[la]) for la in (1, 2))
        n_whole = sum(len(WHOLE[la]) + 2 * (GROUPS - 1 in WHOLE[la]) for la in (1, 2))

        block = ctx.enter_context(nc.Block())

        @block.sync
        def _(sp):
            ids_v = ids.rearrange("(t p) f -> t p f", p=ST)
            dense_v = dense.rearrange("c (t p) -> t c p", p=ST)

            def rights(u, k):
                if not real(u, k):
                    return
                if number(u) and CT * u + k == 0:
                    sp.wait_ge(s_left, 1)
                else:
                    sp.wait_ge(s_z[0], count(3, u, k - 1, 1))
                for g, (a, b) in enumerate(PAIR_GROUPS):
                    for c in range(a, b):
                        for n in range(PAIR_BLOCKS):
                            block = PAIR_BLOCKS * c + n
                            if block <= DISTANCES:
                                j = (block + 1) % (DISTANCES + 1)
                                sp.dma_start(pair_ops[FIELDS * n:FIELDS * (n + 1), 1 + c, :],
                                             pair_ops[j:j + FIELDS, 0, :]).then_inc(s_right[g], 16)

            def load_index(t):
                sp.dma_start(index_sb[:, :], ids_v[t, :, :]).then_inc(s_index, 16)

            load_index(0)
            sp.dma_start(identity_sb[:, :], identity).then_inc(s_const, 16)
            sp.dma_start(select_sb[:, :, :], select).then_inc(s_const, 16)
            full = PAIR_CHUNKS - 1
            sp.dma_start(w0_sb[:, 0:full, :], w0_fwd[0:full * PAIR_ROWS, :].rearrange("(c p) s -> p c s", p=PAIR_ROWS)).then_inc(s_w0, 16)
            sp.dma_start(w0_sb[0:PAIR_TAIL, full, :], w0_fwd[full * PAIR_ROWS:, :]).then_inc(s_w0, 16)
            rev = products[:, 0, :, :].rearrange("p g c -> p (g c)").rearrange("p (c s) -> p c s", s=SIZE)
            sp.dma_start(rev[0:PAIR_ROWS, 0:full, :], w0_rev[0:full * PAIR_ROWS, :].rearrange("(c p) s -> p c s", p=PAIR_ROWS)).then_inc(s_w0, 16)
            sp.dma_start(rev[0:FIELDS, full, :], w0_rev[full * PAIR_ROWS:, :]).then_inc(s_w0, 16)
            sp.dma_start(columns_sb[:, :], columns).then_inc(s_bias, 16)
            for n, (layer, w) in enumerate(((1, w1), (2, w2))):
                stage = products[:, 1 + n, :, :].rearrange("p g c -> p (g c)").rearrange("p (c s) -> p c s", s=SIZE)
                for groups, dst, done in ((SPLIT[layer], stage, s_wstage), (WHOLE[layer], w_whole[layer], s_wwhole)):
                    for i, g in enumerate(groups):
                        have = GROUP if g < GROUPS - 1 else GROUP - 1
                        row = g * GROUP * 128
                        sp.dma_start(dst[:, i * GROUP:i * GROUP + have, :],
                                     w[row:row + 128 * have, :].rearrange("(c p) s -> p c s", p=128)).then_inc(done, 16)
                        if have < GROUP:
                            for p in (0, HALF):
                                sp.dma_start(dst[p:p + TAIL, i * GROUP + have, :], w[row + 128 * have:, :]).then_inc(done, 16)
            sp.wait_ge(s_gathered, 16 * FIELDS)
            load_index(1)
            sp.dma_start(top1_sb[0:HALF, 0, :], w_top1[HALF:SIZE, :]).then_inc(s_top, 16)
            sp.dma_start(top1_sb[HALF:SIZE, 0, :], w_top1[0:HALF, :]).then_inc(s_top, 16)
            sp.dma_start(top1_sb[:, 1, :], w_top1[SIZE:2 * SIZE, :]).then_inc(s_top, 16)
            sp.dma_start(top1_dense_sb[:, :], w_top1[2 * SIZE:, :]).then_inc(s_top, 16)
            sp.dma_start(top2_sb[:, :, :], w_top2.rearrange("(m p) n -> p m n", p=128)).then_inc(s_top, 16)

            sp.wait_ge(s_blank, 1)
            for k in range(3):
                rights(0, k)
            with sp.Fori(0, SAMPLE_TILES - 1) as u:
                for k in range(1, CT + 1):
                    rights(u, k + 2)
                    if k == 1:
                        load_index(u + 2)
                        sp.dma_start(dense_sb[:, :], dense_v[u, :, :]).then_inc(s_dense, 16)
            rights(0, COLUMN_TILES - 1)
            sp.wait_ge(s_h1, SAMPLE_TILES - 1)
            sp.dma_start(dense_sb[:, :], dense_v[SAMPLE_TILES - 1, :, :]).then_inc(s_dense, 16)
            sp.wait_ge(s_yr, SAMPLE_TILES)
            sp.dma_start(out.rearrange("b one -> one b"), y_sb[:, :]).then_inc(s_stored, 16)
            sp.wait_ge(s_stored, 16)

        @block.gpsimd
        def _(pool):
            def gather(fields):
                for f in fields:
                    nc.gpsimd.indirect_dma_start(
                        out=rows_sb[:, f, :], out_offset=None, in_=tables[f],
                        in_offset=bass.IndirectOffsetOnAxis(ap=index_sb[:, f:f + 1], axis=0),
                    ).then_inc(s_gathered, 16)

            def rest(t, n):
                pool.wait_ge(s_part, t * PARTS + n + 1)
                src = rest_sb[:, :, :] if n else rows_sb[:, :, :].rearrange("p f d -> p d f")
                nc.gpsimd.tensor_tensor(rest_sb[:, :, :], src, parts_sb[:, :, n, :], ALU.subtract).then_inc(s_rest, 1)

            def sums(u, k):
                q = k % CT
                for n, direct in enumerate((direct01, direct2)):
                    if n == 0:
                        pool.wait_ge(s_z[0], count(3, u, k, 3))
                        pool.wait_ge(s_z[1], count(3, u, k, 3))
                    else:
                        pool.wait_ge(s_z[2], count(1, u, k, 1))
                    src = direct[:, k % 2, :]
                    half, whole, run = src[:, 0:COLS // 2], src[:, 0:ST], running[:, n, :]
                    nc.gpsimd.tensor_tensor(half, half, src[:, COLS // 2:COLS], ALU.add).then_inc(s_sum, 1)
                    pool.wait_ge(s_sum, count(6, u, k, 3 * n + 1))
                    if q == 0:
                        nc.gpsimd.tensor_tensor(run, whole, half[:, ST:2 * ST], ALU.add).then_inc(s_sum, 2)
                        continue
                    nc.gpsimd.tensor_tensor(whole, whole, half[:, ST:2 * ST], ALU.add).then_inc(s_sum, 1)
                    pool.wait_ge(s_sum, count(6, u, k, 3 * n + 2))
                    if q < CT - 1:
                        nc.gpsimd.tensor_tensor(run, run, whole, ALU.add).then_inc(s_sum, 1)
                    else:
                        nc.gpsimd.tensor_tensor(features[:, n, :], run, whole, ALU.add).then_inc(s_sum, 1)

            def pair_products(u, k):
                if not real(u, k):
                    return
                for g, (a, b) in enumerate(PAIR_GROUPS):
                    blocks = min(PAIR_BLOCKS * b, DISTANCES + 1) - PAIR_BLOCKS * a
                    pool.wait_ge(s_right[g], count(16 * blocks, u, k, 16 * blocks))
                    left = pair_ops[0:PAIR_ROWS, 0:1, :].broadcast_to([PAIR_ROWS, b - a, COLS])
                    right = pair_ops[0:PAIR_ROWS, 1 + a:1 + b, :]
                    nc.gpsimd.tensor_tensor(right, left, right, ALU.mult).then_inc(s_prod[0], 1)

            nc.gpsimd.memset(pair_ops[:, PAIR_CHUNKS, :], 0.0).then_inc(s_blank, 1)
            pool.wait_ge(s_index, 16)
            gather(range(FIELDS))
            rest(0, 0)
            rest(0, 1)
            pool.wait_ge(s_index, 2 * 16)
            pool.wait_ge(s_part, PARTS)
            gather(range(2 * GATHERS))
            pair_products(0, 1)
            gather(range(2 * GATHERS, FIELDS))
            with pool.Fori(0, SAMPLE_TILES - 1) as u:
                for k in range(1, CT + 1):
                    pair_products(u, k + 1)
                    if k == 1:
                        rest(u + 1, 0)
                    sums(u, k - 1)
                    if k == 1:
                        rest(u + 1, 1)
                        pool.wait_ge(s_index, (u + 3) * 16)
                        pool.wait_ge(s_part, (u + 2) * PARTS)
                    else:
                        gather(range((k - 2) * GATHERS, (k - 1) * GATHERS))
            for k in range(COLUMN_TILES - CT + 1, COLUMN_TILES + 1):
                pair_products(0, k + 1)
                sums(0, k - 1)
            pool.wait_ge(s_gathered, 16 * FIELDS * (SAMPLE_TILES + 1))

        @block.tensor
        def _(pe):
            def transposes(u, t, h):
                buffer, taken, value = selection_buffer("parts", u, t, h)
                pe.wait_ge(s_part, (u + t) * PARTS + PARTS)
                if taken is not None:
                    pe.wait_ge(taken, value)
                dst = sel_ps[:, buffer, 0, :].bitcast(bf16)
                for d in range(DIM // 2):
                    last = nc.tensor.transpose(
                        dst[0:STACK, d * ST:(d + 1) * ST],
                        parts_sb[:, h * (DIM // 2) + d, :, :].rearrange("p s f -> p (s f)"), identity_sb[:, :])
                last.then_inc(s_transposed, 1)

            def select_left(u, k):
                if not real(u, k):
                    return
                buffer, taken, value = selection_buffer("left", u, k, 0)
                if taken is not None:
                    pe.wait_ge(taken, value)
                if k % 2 == 0:
                    pe.wait_ge(s_stacked, u * 2 + (k // 2 + 1))
                nc.tensor.matmul(sel_ps[:, buffer, 0, :], select_sb[:, 0, :], stacked[:, k % CT, :],
                                 start=True, stop=True).then_inc(s_left_made, 1)

            def select_rows(u, k, i):
                if not real(u, k):
                    return
                buffer, taken, value = selection_buffer("rows", u, k, i)
                pe.wait_ge(taken, value)
                for n in range(2):
                    last = nc.tensor.matmul(sel_ps[:, buffer, n, :], select_sb[:, 1 + 2 * i + n, :],
                                            stacked[:, k % CT, :], start=True, stop=True)
                last.then_inc(s_bc_made, 1)

            def contract(u, k, layer, g):
                if not real(u, k):
                    return
                z = z_ps[:, layer, :]
                if g == 0:
                    wait(pe, s_z[layer], count({0: 3, 1: 3, 2: 1}[layer], u, k, 0))
                    if layer < 2:
                        wait(pe, s_prod[layer + 1], count(GROUPS, u, k, 0))
                if layer == 0:
                    pe.wait_ge(s_prod[0], count(PER_TILE[0], u, k, g + 1))
                    for c in range(*PAIR_GROUPS[g]):
                        rows = PAIR_ROWS if c < PAIR_CHUNKS - 1 else PAIR_TAIL
                        last = nc.tensor.matmul(z, w0_sb[0:rows, c, :], pair_ops[0:rows, 1 + c, :],
                                                start=(c == 0), stop=(c == PAIR_CHUNKS - 1))
                elif g in WHOLE[layer]:
                    buffer = buffer_of(WORK, RING, k, (layer, g))
                    pe.wait_ge(s_prod[layer], count(GROUPS, u, k, g + 1))
                    for n in range(GROUP):
                        c = GROUP * g + n
                        rows = 128 if c < CHUNKS - 1 else TAIL
                        last = nc.tensor.matmul(z, w_whole[layer][0:rows, WHOLE[layer].index(g) * GROUP + n, :],
                                                products[0:rows, buffer, n, :],
                                                start=(c == 0), stop=(c == CHUNKS - 1))
                else:
                    i = SPLIT[layer].index(g)
                    buffer = buffer_of(SPLIT_WORK, SPLIT_RING, k, (layer, g))
                    rows = [128 if GROUP * g + n < CHUNKS - 1 else TAIL for n in range(GROUP)]
                    pe.wait_ge(s_high[layer], count(len(SPLIT[layer]), u, k, i + 1))
                    for n, p in enumerate(rows):
                        c = i * GROUP + n
                        high = prod_high[0:p, buffer, n, :]
                        nc.tensor.matmul(z, w_high[layer][0:p, c, :], high, start=(g == 0 and n == 0), stop=False)
                        last = nc.tensor.matmul(z, w_low[layer][0:p, c, :], high, start=False, stop=False)
                    last.then_inc(s_used[layer], 1)
                    pe.wait_ge(s_low[layer], count(len(SPLIT[layer]), u, k, i + 1))
                    for n, p in enumerate(rows):
                        last = nc.tensor.matmul(z, w_high[layer][0:p, i * GROUP + n, :], prod_low[0:p, buffer, n, :],
                                                start=False, stop=(g == GROUPS - 1 and n == GROUP - 1))
                last.then_inc(s_mm[layer], 1)

            def mlp1(t):
                pe.wait_ge(s_sum, t * (6 * CT) + 6 * CT)
                pe.wait_ge(s_dense, t * 16 + 16)
                for m in range(HID1 // 128):
                    cols = slice(m * 128, (m + 1) * 128)
                    nc.tensor.matmul(top_ps[:, cols], top1_sb[:, 0, cols], features[:, 0, :], start=True, stop=False)
                    nc.tensor.matmul(top_ps[:, cols], top1_sb[:, 1, cols], features[:, 1, :], start=False, stop=False)
                    last = nc.tensor.matmul(top_ps[:, cols], top1_dense_sb[:, cols], dense_sb[:, :], start=False, stop=True)
                last.then_inc(s_h1, 1)

            def mlp2(t):
                pe.wait_ge(s_h1r, t * (HID1 // 128) + HID1 // 128)
                for m in range(HID2 // 128):
                    cols = slice(m * 128, (m + 1) * 128)
                    for c in range(HID1 // 128):
                        last = nc.tensor.matmul(top_ps[:, cols], top2_sb[:, c, cols], hidden1[:, c, :],
                                                start=(c == 0), stop=(c == HID1 // 128 - 1))
                last.then_inc(s_h2, 1)

            def mlp3(t):
                pe.wait_ge(s_h2r, t * (HID2 // 128) + HID2 // 128)
                for c in range(HID2 // 128):
                    last = nc.tensor.matmul(top_ps[0:1, 0:ST], top3_sb[:, c:c + 1], hidden2[:, c, :],
                                            start=(c == 0), stop=(c == HID2 // 128 - 1))
                last.then_inc(s_y, 1)

            def mlp(u, k, layer):
                if k % CT == 0 and k > 0:
                    layer(u + (k // CT - 1))

            def period(u, k):
                for g in (0, 1, 2):
                    contract(u, k, 1, g)
                select_left(u, k + 2)
                contract(u, k, 1, 3)
                contract(u, k, 1, 4)
                select_rows(u, k + 1, 0)
                select_rows(u, k + 1, 1)
                contract(u, k + 1, 0, 0)
                contract(u, k + 1, 0, 1)
                mlp(u, k, mlp1)
                contract(u, k, 2, 0)
                select_rows(u, k + 1, 2)
                contract(u, k, 2, 1)
                select_rows(u, k + 1, 3)
                select_rows(u, k + 1, 4)
                mlp(u, k, mlp2)
                contract(u, k, 2, 2)
                select_rows(u, k + 1, 5)
                select_rows(u, k + 1, 6)
                contract(u, k, 2, 3)
                select_rows(u, k + 1, 7)
                mlp(u, k, mlp3)
                contract(u, k, 2, 4)
                select_rows(u, k + 1, 8)
                select_rows(u, k + 1, 9)
                if k > 0 and k % 2 and k // CT + 1 < SAMPLE_TILES:
                    transposes(u, k // CT + 1, k % CT // 2)

            pe.wait_ge(s_const, 2 * 16)
            transposes(0, 0, 0)
            transposes(0, 0, 1)
            select_left(0, 0)
            pe.wait_ge(s_wprep, 2)
            period(0, -1)
            pe.wait_ge(s_wprep, n_prep)
            pe.wait_ge(s_wwhole, n_whole * 16)
            period(0, 0)
            pe.wait_ge(s_top, 5 * 16)
            with pe.Fori(0, SAMPLE_TILES - 1) as u:
                for k in range(1, CT + 1):
                    period(u, k)
            for k in range(COLUMN_TILES - CT + 1, COLUMN_TILES):
                period(0, k)
            mlp1(SAMPLE_TILES - 1)
            mlp2(SAMPLE_TILES - 1)
            mlp3(SAMPLE_TILES - 1)

        @block.vector
        def _(dve):
            def product(u, k, layer, g):
                tile, (la, gb) = user_before(WORK, RING, k, (layer, g))
                if gb in WHOLE[la]:
                    wait(dve, s_mm[la], count(GROUPS, u, tile, gb + 1))
                else:
                    wait(dve, s_low[la], count(len(SPLIT[la]), u, tile, SPLIT[la].index(gb) + 1))
                if layer == 1:
                    dve.wait_ge(s_bc_ready, count(BC_ITEMS, u, k, 2 * g + 2))
                if g == 0:
                    dve.wait_ge(s_z[layer - 1], count(3, u, k, 3))
                xk = z_ps[:, layer - 1:layer, :].broadcast_to([128, GROUP, COLS])
                nc.vector.tensor_tensor(products[:, buffer_of(WORK, RING, k, (layer, g)), :, :],
                                        x0_rows[:, GROUP * g:GROUP * (g + 1), :], xk, ALU.mult).then_inc(s_prod[layer], 1)

            def low(u, k, layer, g):
                buffer = buffer_of(SPLIT_WORK, SPLIT_RING, k, (layer, g))
                tile, (la, gb) = user_before(SPLIT_WORK, SPLIT_RING, k, (layer, g))
                wait(dve, s_mm[la], count(GROUPS, u, tile, gb + 1))
                dve.wait_ge(s_high[layer], count(len(SPLIT[layer]), u, k, SPLIT[layer].index(g) + 1))
                nc.vector.tensor_tensor(prod_low[:, buffer, :, :], products[:, buffer_of(WORK, RING, k, (layer, g)), :, :],
                                        prod_high[:, buffer, :, :].bitcast(f32), ALU.subtract).then_inc(s_low[layer], 1)

            def period(u, k):
                for g in (0, 1, 2, 3):
                    product(u, k, 1, g)
                low(u, k, 1, 2)
                product(u, k, 1, 4)
                low(u, k, 1, 3)
                low(u, k, 1, 4)
                for g in (0, 1, 2):
                    product(u, k, 2, g)
                low(u, k, 2, 1)
                product(u, k, 2, 3)
                low(u, k, 2, 2)
                low(u, k, 2, 3)
                product(u, k, 2, 4)

            full = PAIR_CHUNKS - 1
            rev = products[:, 0, :, :].rearrange("p g c -> p (g c)").rearrange("p (c s) -> p c s", s=SIZE)
            dve.wait_ge(s_w0, 4 * 16)
            nc.vector.tensor_tensor(w0_sb[:, 0:full, :], w0_sb[:, 0:full, :], rev[0:PAIR_ROWS, 0:full, :], ALU.add).then_inc(s_wprep, 1)
            nc.vector.tensor_tensor(w0_sb[0:FIELDS, full, :], w0_sb[0:FIELDS, full, :], rev[0:FIELDS, full, :], ALU.add).then_inc(s_wprep, 1)
            dve.wait_ge(s_wstage, n_stage * 16)
            for n, layer in enumerate((1, 2)):
                stage = products[:, 1 + n, :, :].rearrange("p g c -> p (g c)").rearrange("p (c s) -> p c s", s=SIZE)[:, 0:len(SPLIT[layer]) * GROUP, :]
                nc.vector.tensor_copy(w_high[layer][:, :, :], stage).then_inc(s_wprep, 1)
                dve.wait_ge(s_wprep, 2 + 2 * n + 1)
                nc.vector.tensor_tensor(w_low[layer][:, :, :], stage, w_high[layer][:, :, :].bitcast(f32), ALU.subtract).then_inc(s_wprep, 1)
            dve.wait_ge(s_wprep, n_prep)
            for g, (a, b) in enumerate(PAIR_GROUPS):
                blocks = min(PAIR_BLOCKS * b, DISTANCES + 1) - PAIR_BLOCKS * a
                dve.wait_ge(s_right[g], 16 * blocks)
                left = pair_ops[0:PAIR_ROWS, 0:1, :].broadcast_to([PAIR_ROWS, b - a, COLS])
                right = pair_ops[0:PAIR_ROWS, 1 + a:1 + b, :]
                nc.vector.tensor_tensor(right, left, right, ALU.mult).then_inc(s_prod[0], 1)
            period(0, 0)
            with dve.Fori(0, SAMPLE_TILES - 1) as u:
                for k in range(1, CT + 1):
                    period(u, k)
            for k in range(COLUMN_TILES - CT + 1, COLUMN_TILES):
                period(0, k)

        @block.scalar
        def _(act):
            def part(t, n):
                if n == 0:
                    act.wait_ge(s_gathered, (t + 1) * (16 * FIELDS))
                    wait(act, s_transposed, t * 2)
                    src = rows_sb[:, :, :].rearrange("p f d -> p d f")
                else:
                    act.wait_ge(s_rest, t * (PARTS - 1) + n)
                    src = rest_sb[:, :, :]
                nc.scalar.activation(parts_sb[:, :, n, :], src, ACT.Copy).then_inc(s_part, 1)

            def take_transposed(u, t, h):
                buffer, _, _ = selection_buffer("parts", u, t, h)
                act.wait_ge(s_transposed, (u + t) * 2 + h + 1)
                nc.scalar.activation(stacked[:, 2 * h:2 * h + 2, :].rearrange("p q c -> p (q c)"),
                                     sel_ps[:, buffer, 0, :].bitcast(bf16)[0:STACK, :], ACT.Copy).then_inc(s_stacked, 1)

            def take_left(u, k):
                if not real(u, k):
                    return
                buffer, _, _ = selection_buffer("left", u, k, 0)
                act.wait_ge(s_left_made, count(1, u, k, 1))
                wait(act, s_prod[0], count(PER_TILE[0], u, k, 0))
                nc.scalar.activation(pair_ops[:, 0, :], sel_ps[:, buffer, 0, :], ACT.Copy).then_inc(s_left, 1)

            def take_rows(u, k, i):
                if not real(u, k):
                    return
                buffer, _, _ = selection_buffer("rows", u, k, i)
                act.wait_ge(s_bc_made, count(BC_ITEMS, u, k, i + 1))
                if i % 2 == 0:
                    wait(act, s_prod[2], count(GROUPS, u, k - 1, i // 2 + 1))
                nc.scalar.activation(x0_rows[:, 2 * i:2 * i + 2, :], sel_ps[:, buffer, :, :], ACT.Copy).then_inc(s_bc_ready, 1)

            def high(u, k, layer, g):
                tile, (la, gb) = user_before(SPLIT_WORK, SPLIT_RING, k, (layer, g))
                wait(act, s_used[la], count(len(SPLIT[la]), u, tile, SPLIT[la].index(gb) + 1))
                act.wait_ge(s_prod[layer], count(GROUPS, u, k, g + 1))
                nc.scalar.activation(prod_high[:, buffer_of(SPLIT_WORK, SPLIT_RING, k, (layer, g)), :, :],
                                     products[:, buffer_of(WORK, RING, k, (layer, g)), :, :], ACT.Copy).then_inc(s_high[layer], 1)

            def relu(dst, src, bias, done):
                nc.scalar.activation(dst, src, ACT.Relu, bias=bias).then_inc(done, 1)

            def take_z(u, k, layer):
                if not real(u, k):
                    return
                act.wait_ge(s_mm[layer], count(PER_TILE[layer], u, k, PER_TILE[layer]))
                z, bias = z_ps[:, layer, :], bias_sb[:, layer:layer + 1]
                summed = k - 2 if number(u) or k >= 2 else k - 1
                if layer < 2:
                    dst = direct01[HALF:SIZE, k % 2, :] if layer == 0 else direct01[0:HALF, k % 2, :]
                    wait(act, s_sum, count(6, u, summed, 3))
                    relu(dst, z[HALF:SIZE, :], bias[HALF:SIZE, :], s_z[layer])
                    act.wait_ge(s_z[layer], count(3, u, k, 1))
                    relu(z[HALF:SIZE, :], z[0:HALF, :], bias[0:HALF, :], s_z[layer])
                    act.wait_ge(s_z[layer], count(3, u, k, 2))
                    relu(z[0:HALF, :], z[0:HALF, :], bias[0:HALF, :], s_z[layer])
                else:
                    wait(act, s_sum, count(6, u, summed, 6))
                    relu(direct2[:, k % 2, :], z, bias, s_z[2])

            def mlp_relu1(t):
                act.wait_ge(s_h1, t + 1)
                for m in range(HID1 // 128):
                    relu(hidden1[:, m, :], top_ps[:, m * 128:(m + 1) * 128], bias_top1_sb[:, m:m + 1], s_h1r)

            def mlp_relu2(t):
                act.wait_ge(s_h2, t + 1)
                for m in range(HID2 // 128):
                    relu(hidden2[:, m, :], top_ps[:, m * 128:(m + 1) * 128], bias_top2_sb[:, m:m + 1], s_h2r)

            def mlp_out(t):
                act.wait_ge(s_y, t + 1)
                nc.scalar.activation(y_sb[:, bass.ds(t * ST, ST)], top_ps[0:1, 0:ST], ACT.Copy).then_inc(s_yr, 1)

            def mlp(u, k, step):
                if k % CT == 0 and k > 0:
                    step(u + (k // CT - 1))

            def next_part(u, k, n):
                if k > 0 and k % CT == 1 and k // CT + 1 < SAMPLE_TILES:
                    part(u + (k // CT + 1), n)

            def period(u, k):
                if real(u, k):
                    for g in (2, 3, 4):
                        high(u, k, 1, g)
                next_part(u, k, 0)
                take_left(u, k + 2)
                take_z(u, k, 1)
                take_rows(u, k + 1, 0)
                take_rows(u, k + 1, 1)
                next_part(u, k, 1)
                if real(u, k):
                    high(u, k, 2, 1)
                take_z(u, k + 1, 0)
                mlp(u, k, mlp_relu1)
                if real(u, k):
                    high(u, k, 2, 2)
                take_rows(u, k + 1, 2)
                next_part(u, k, 2)
                if real(u, k):
                    high(u, k, 2, 3)
                take_rows(u, k + 1, 3)
                take_rows(u, k + 1, 4)
                mlp(u, k, mlp_relu2)
                for i in (5, 6, 7):
                    take_rows(u, k + 1, i)
                mlp(u, k, mlp_out)
                take_z(u, k, 2)
                take_rows(u, k + 1, 8)
                take_rows(u, k + 1, 9)
                if k > 0 and k % 2 and k // CT + 1 < SAMPLE_TILES:
                    take_transposed(u, k // CT + 1, k % CT // 2)

            act.wait_ge(s_bias, 16)
            for n in range(PARTS):
                part(0, n)
            take_transposed(0, 0, 0)
            take_transposed(0, 0, 1)
            take_left(0, 0)
            period(0, -1)
            period(0, 0)
            with act.Fori(0, SAMPLE_TILES - 1) as u:
                for k in range(1, CT + 1):
                    period(u, k)
            for k in range(COLUMN_TILES - CT + 1, COLUMN_TILES):
                period(0, k)
            mlp_relu1(SAMPLE_TILES - 1)
            mlp_relu2(SAMPLE_TILES - 1)
            mlp_out(SAMPLE_TILES - 1)


def pair_order():
    h = np.tile(np.arange(FIELDS), DISTANCES + 1)
    j = np.repeat(np.append(np.arange(1, DISTANCES + 1), 0), FIELDS)
    return h, (h + j) % FIELDS


def selection():
    want = np.full((1 + CHUNKS, 128), -1)
    want[0, :PAIR_ROWS] = np.tile(np.arange(FIELDS), PAIR_BLOCKS)
    want[1:] = np.minimum(np.arange(CHUNKS * 128) // HALF, FIELDS - 1).reshape(CHUNKS, 128)
    return (np.arange(STACK)[:, None, None] % FIELDS == want[None]).astype(np.float32)


def kernel(**inputs):
    import ml_dtypes
    import concourse.bacc as bacc
    from concourse.bass_utils import run_bass_kernel_spmd

    a = {name: np.ascontiguousarray(x) for name, x in inputs.items()}
    left, right = pair_order()
    w0 = a["L0_rec_w0"]
    arrays = {
        "dense": np.ascontiguousarray(a["dense_ctx"].T),
        "ids": np.concatenate([a["ids"], np.zeros((ST, FIELDS), a["ids"].dtype)]),
        "w0_fwd": w0[left, right],
        "w0_rev": w0[right, left][:DISTANCES * FIELDS],
        "w1": a["L0_rec_w1"].reshape(ROWS, SIZE),
        "w2": a["L0_rec_w2"].reshape(ROWS, SIZE),
        "w_top1": a["W_top1"], "w_top2": a["W_top2"],
        "columns": np.concatenate([a[n].reshape(-1, 128) for n in ("L0_rec_b0", "L0_rec_b1", "L0_rec_b2", "b_top1", "b_top2", "W_top3")]).T,
        "select": selection().astype(ml_dtypes.bfloat16),
        "identity": np.eye(128, dtype=ml_dtypes.bfloat16),
    }
    for f in range(FIELDS):
        arrays[f"tbl_{f}"] = a[f"tbl_{f}"]
    arrays = {f"in_{name}": np.ascontiguousarray(x) for name, x in arrays.items()}

    nc = bacc.Bacc("TRN2", target_bir_lowering=False, num_devices=1)
    ap = {name[3:]: nc.dram_tensor(name, x.shape, mybir.dt.from_np(x.dtype), kind="ExternalInput").ap()
          for name, x in arrays.items()}
    out = nc.dram_tensor("out_y", (BATCH, 1), mybir.dt.float32, kind="ExternalOutput").ap()
    build(nc, tables=[ap.pop(f"tbl_{f}") for f in range(FIELDS)], out=out, **ap)
    r = run_bass_kernel_spmd(nc, [arrays], core_ids=[0])
    return r.results[0]["out_y"]
```
